# Optimizing a Trainium2 kernel written in Bass

```python
import numpy as np
import jax
import jax.numpy as jnp

def _softmax(x, axis=-1):
    return jax.nn.softmax(x, axis=axis)

def _gelu(x):
    return jax.nn.gelu(x, approximate=True)

def _silu(x):
    return jax.nn.silu(x)

def _sigmoid(x):
    return jax.nn.sigmoid(x)

def _layernorm(x, axis=-1, eps=1e-05):
    m = jnp.mean(x, axis=axis, keepdims=True)
    v = jnp.var(x, axis=axis, keepdims=True)
    return (x - m) / jnp.sqrt(v + eps)

def _scatter_add(tgt, idx, src, axis=0):
    return tgt.at[idx].add(src)

def _segment_sum(src, seg, n):
    return jax.ops.segment_sum(src, seg, n)
kernel_name = 'mk_conv_preact_d1_conv_nchw128_r4_500d5d'

def setup_inputs(seed: int=0):
    np.random.seed(seed)
    _w = jnp.asarray

    def _rec_inputs():
        import jax
        import jax.numpy as jnp
        _gk = jax.random.key(seed)
        x = 7.22e-05 + 1 * jax.random.normal(jax.random.fold_in(_gk, 1), (16, 32, 16, 16), jnp.float32)
        return x
    x = _rec_inputs()

    def _L0_conv_setup():
        import jax, jax.numpy as jnp
        import numpy as np
        from jax import lax
        K = 4
        OUT_PLANES = 32
        TEMPERATURE = 30.0
        key = jax.random.key(seed)
        ks = jax.random.split(key, 5)
        in_planes, k = (32, 3)
        he_std = float(np.sqrt(2.0)) * (in_planes * k * k) ** (-0.5)
        return {'x': jax.random.normal(ks[0], (16, in_planes, 16, 16), jnp.float32), 'weight': jax.random.normal(ks[1], (K * OUT_PLANES, in_planes, k, k), jnp.float32) * he_std, 'bias': jax.random.normal(ks[2], (K * OUT_PLANES,), jnp.float32) * 0.01, 'se_w1': jax.random.normal(ks[3], (33, in_planes), jnp.float32) * (2.0 / 33) ** 0.5, 'se_w2': jax.random.normal(ks[4], (K, 33), jnp.float32) * (2.0 / K) ** 0.5, 'se_b2': jnp.zeros((K,), jnp.float32)}
    _L0_conv_all = _L0_conv_setup()
    _L0_conv_in = {k: v for k, v in _L0_conv_all.items() if k in ('weight', 'bias', 'se_w1', 'se_w2', 'se_b2')}
    del _L0_conv_all
    return {'x': x, 'L0_conv_weight': _L0_conv_in['weight'], 'L0_conv_bias': _L0_conv_in['bias'], 'L0_conv_se_w1': _L0_conv_in['se_w1'], 'L0_conv_se_w2': _L0_conv_in['se_w2'], 'L0_conv_se_b2': _L0_conv_in['se_b2']}

def reference(x, L0_conv_weight, L0_conv_bias, L0_conv_se_w1, L0_conv_se_w2, L0_conv_se_b2):
    import jax
    import jax.numpy as jnp

    def _L0_conv_ref(x, weight, bias, se_w1, se_w2, se_b2):
        import jax, jax.numpy as jnp
        import numpy as np
        from jax import lax
        K = 4
        OUT_PLANES = 32
        TEMPERATURE = 30.0
        B = x.shape[0]
        pooled = x.mean(axis=(2, 3))
        h = jax.nn.relu(pooled @ se_w1.T)
        logits = h @ se_w2.T + se_b2
        attn = jax.nn.softmax(logits / TEMPERATURE, axis=1)
        y = lax.conv_general_dilated(x, weight, window_strides=(1, 1), padding=[(1, 1), (1, 1)], dimension_numbers=('NCHW', 'OIHW', 'NCHW'))
        y = y + bias[None, :, None, None]
        Ho, Wo = (y.shape[2], y.shape[3])
        y = y.reshape(B, K, OUT_PLANES, Ho, Wo)
        return jnp.einsum('bk,bkohw->bohw', attn, y)

    def _gn(v, G=32, eps=1e-05):
        B_, C_, H_, W_ = v.shape
        g = v.reshape(B_, G, C_ // G, H_, W_)
        m = jnp.mean(g, axis=(2, 3, 4), keepdims=True)
        s = jnp.var(g, axis=(2, 3, 4), keepdims=True)
        return ((g - m) / jnp.sqrt(s + eps)).reshape(v.shape)

    def _ln_c(v, eps=1e-06):
        m = jnp.mean(v, axis=1, keepdims=True)
        s = jnp.var(v, axis=1, keepdims=True)
        return (v - m) / jnp.sqrt(s + eps)

    def _ln_t(v, eps=1e-05):
        m = jnp.mean(v, axis=-1, keepdims=True)
        s = jnp.var(v, axis=-1, keepdims=True)
        return (v - m) / jnp.sqrt(s + eps)

    def _to_tokens(v):
        B_, C_, H_, W_ = v.shape
        return v.reshape(B_, C_, H_ * W_).transpose(0, 2, 1)

    def _from_tokens(t, like):
        B_, C_, H_, W_ = like.shape
        return t.transpose(0, 2, 1).reshape(B_, C_, H_, W_)
    x = x + _L0_conv_ref(_gn(x), L0_conv_weight, L0_conv_bias, L0_conv_se_w1, L0_conv_se_w2, L0_conv_se_b2)
    return x

_drawn_inputs = setup_inputs


def setup_inputs(seed=0):
    import zlib

    import numpy as np

    out = dict(_drawn_inputs(seed))
    spreads = {'L0_conv_se_b2': (0.0, 0.8)}
    factors = {'L0_conv_bias': 8.0}
    for name, (base, spread) in spreads.items():
        noise = np.random.default_rng([zlib.crc32(name.encode()), seed]).standard_normal(out[name].shape)
        drawn = base * np.exp(spread * noise) if base else spread * noise
        out[name] = jnp.asarray(drawn.astype(out[name].dtype))
    for name, factor in factors.items():
        out[name] = (out[name] * factor).astype(out[name].dtype)
    return out
```

```python
from contextlib import ExitStack

import concourse.bass as bass
from concourse import mybir

F32 = mybir.dt.float32
ALU = mybir.AluOpType
ACT = mybir.ActivationFunctionType
AX_X = mybir.AxisListType.X

GN_EPS = 1e-5
TEMPERATURE = 30.0


def repeat(ap, axis, n):
    longer = ap.unsqueeze(axis)
    shape = list(longer.shape)
    shape[axis] = n
    return longer.broadcast_to(shape)


def preact_dynamic_conv(nc: bass.Bass, x, weight, bias, se_w1, se_w2, se_b2, out):
    B, C, H, W = x.shape
    KO, _, KH, KW = weight.shape
    HID = se_w1.shape[0]
    K = se_w2.shape[0]
    O = KO // K
    PIX = H * W
    P = 128
    QUADS = P // C
    ROUNDS = B // QUADS
    STACK = KH * C
    PADW = W + 2
    HALVES = 2
    BH = B // HALVES
    assert C == 32 and O == 32 and KO == P and KH == 3 and KW == 3 and P % C == 0 and HID < 63

    x_nat_dram = x.rearrange("(g j) c h w -> (j c) g (h w)", g=ROUNDS)
    out_dram = out.rearrange("(g j) c h w -> (j c) g (h w)", g=ROUNDS)
    x_chan_dram = x.rearrange("b c h w -> c b (h w)")
    w_dram = weight.rearrange("n c kh kw -> n (c kh kw)")

    ctx = ExitStack()
    with ctx:
        def sb(name, shape):
            return ctx.enter_context(nc.sbuf_tensor(name, shape, F32))

        def pb(name, shape):
            return ctx.enter_context(nc.psum_tensor(name, shape, F32))

        def sem(name):
            return ctx.enter_context(nc.semaphore(name))

        x_nat = sb("x_nat", [P, ROUNDS, PIX])
        x_raw = sb("x_raw", [STACK, B, PIX])
        x_pad = sb("x_pad", [P, B, H, PADW])
        y_sb = sb("y_sb", [P, ROUNDS, PIX])
        w_raw = sb("w_raw", [P, C * KH * KW])
        bias_col = sb("bias_col", [P, 1])
        w1_rep = sb("w1_rep", [HID, QUADS, C])
        w2_ext = sb("w2_ext", [K, HID + 1])
        ident = sb("ident", [P, P])
        diag_c = sb("diag_c", [P, C])
        in_quad = sb("in_quad", [P, QUADS])
        pick_chan = sb("pick_chan", [P, STACK])
        expert_rows = sb("expert_rows", [K, P])
        ones = sb("ones", [HID + 1, P])
        minus_half = sb("minus_half", [P, ROUNDS])
        w_stack = sb("w_stack", [P, KW, P])
        w1_t = sb("w1_t", [P, HID])
        w2_t = sb("w2_t", [HID + 1, P])
        bn_raw = sb("bn_raw", [P, ROUNDS, 6])
        x_sum = sb("x_sum", [P, ROUNDS])
        MEAN, RSTD, NBIAS, POOLED = range(4)
        stat = sb("stat", [P, 4, ROUNDS])
        resid_mean = sb("resid_mean", [P, ROUNDS])
        stat_by_quad = sb("stat_by_quad", [P, 4, ROUNDS, QUADS])
        stat_rep = sb("stat_rep", [STACK, 3, B])
        hidden = sb("hidden", [HID + 1, B])
        hidden_w2 = sb("hidden_w2", [HID + 1, K, B])
        top = sb("top", [P, B])
        below_top = sb("below_top", [P, K + 1, B])
        e_all = sb("e_all", [P, K + 1, B])
        e_sum = sb("e_sum", [P, B])
        e_rsum = sb("e_rsum", [P, ROUNDS, QUADS])
        e_rsum_quad = sb("e_rsum_quad", [P, ROUNDS, QUADS])
        out_scale = sb("out_scale", [P, ROUNDS])
        attn_diag = sb("attn_diag", [P, B, O])
        mixed = sb("mixed", [P, KW, B, O])

        mix_ps = pb("mix_ps", [P, KW, 512])
        conv_ps = pb("conv_ps", [P, ROUNDS, 512])
        logit_ps = pb("logit_ps", [P, 512])
        w1t_ps = conv_ps[:, 0, 0:HID]
        hidden_ps = conv_ps[0:HID, 0, 64:64 + B]
        w2t_ps = conv_ps[0:HID + 1, 1, 0:P]
        stat_ps = conv_ps[0:STACK, 2, 0:3 * B]
        logits = logit_ps[:, 0:(K + 1) * B]

        nat_in = [sem(f"nat_in{g}") for g in range(ROUNDS)]
        raw_in = [sem(f"raw_in{g}") for g in range(ROUNDS)]
        w1_in = sem("w1_in")
        w2_in = sem("w2_in")
        w_in = sem("w_in")
        bias_in = sem("bias_in")
        ident_zero = sem("ident_zero")
        ident_ready = sem("ident_ready")
        raw_edge_ready = sem("raw_edge_ready")
        pool_consts = sem("pool_consts")
        pad_ready = sem("pad_ready")
        w_stack_zero = sem("w_stack_zero")
        w_stack_ready = sem("w_stack_ready")
        masks_ready = sem("masks_ready")
        w1t_done = sem("w1t_done")
        w1t_ready = sem("w1t_ready")
        w2t_done = sem("w2t_done")
        w2t_ready = sem("w2t_ready")
        sums_ready = sem("sums_ready")
        bn_ready = sem("bn_ready")
        aggr_ready = sem("aggr_ready")
        vareps_ready = sem("vareps_ready")
        rstd_ready = sem("rstd_ready")
        chain = sem("chain")
        pooled_ready = sem("pooled_ready")
        stat_ready = sem("stat_ready")
        hidden_done = sem("hidden_done")
        stat_done = sem("stat_done")
        stat_rep_ready = sem("stat_rep_ready")
        hidden_ready = sem("hidden_ready")
        hidden_w2_ready = sem("hidden_w2_ready")
        logits_done = sem("logits_done")
        below_top_ready = sem("below_top_ready")
        e_ready = sem("e_ready")
        diag_ready = sem("diag_ready")
        mix_done = sem("mix_done")
        mixed_by_act = sem("mixed_by_act")
        mixed_by_dve = sem("mixed_by_dve")
        norm_by_act = sem("norm_by_act")
        norm_by_dve = sem("norm_by_dve")
        edge_zero = sem("edge_zero")
        conv_done = sem("conv_done")
        y_ready = sem("y_ready")
        y_out = sem("y_out")

        def quad_of(r):
            return slice(QUADS * r, QUADS * (r + 1))

        def load_raw(eng, r):
            for dy in range(KH):
                lo, hi = max(0, 1 - dy) * W, (H - max(0, dy - 1)) * W
                move = (dy - 1) * W
                eng.dma_start(x_raw[dy * C:(dy + 1) * C, quad_of(r), lo:hi],
                              x_chan_dram[:, quad_of(r), lo + move:hi + move]).then_inc(raw_in[r], 16)

        def evacuated_by_act(piece):
            return piece % KW != 1

        ACT_NORM = (0, 2)
        DVE_NORM = (1, 3)

        def mix_cols(piece):
            half, dx = divmod(piece, KW)
            return dx, slice(BH * half, BH * (half + 1)), slice(BH * O * half, BH * O * (half + 1))

        block = ctx.enter_context(nc.Block())

        @block.sync
        def _(sp):
            for g in range(ROUNDS):
                sp.dma_start(x_nat[:, g, :], x_nat_dram[:, g, :]).then_inc(nat_in[g], 16)
            for r in range(ROUNDS):
                load_raw(sp, r)
            for r in range(ROUNDS):
                sp.wait_ge(y_ready, r + 1)
                sp.dma_start(out_dram[:, r, :], y_sb[:, r, :]).then_inc(y_out, 16)
            sp.wait_ge(y_out, 16 * ROUNDS)

        @block.gpsimd
        def _(pool):
            nc.gpsimd.memset(ident[:], 0.0).then_inc(ident_zero, 1)
            pool.wait_ge(ident_zero, 1)
            nc.gpsimd.affine_select(out=ident[:], in_=ident[:], compare_op=ALU.not_equal, fill=1.0, base=0,
                                    pattern=[[-1, P]], channel_multiplier=1).then_inc(ident_ready, 1)
            nc.gpsimd.memset(ones[:], 1.0).then_inc(pool_consts, 1)
            nc.gpsimd.memset(hidden[:], 1.0).then_inc(pool_consts, 1)
            nc.gpsimd.memset(minus_half[:], -0.5).then_inc(pool_consts, 1)
            nc.gpsimd.memset(w_stack[:, :, STACK:P], 0.0).then_inc(w_stack_zero, 1)
            pool.wait_ge(w_in, 16)
            nc.gpsimd.tensor_copy(w_stack[:, :, 0:STACK].rearrange("p dx (dy c) -> p dx dy c", dy=KH),
                                  w_raw[:].rearrange("p (c dy dx) -> p dx dy c", dy=KH, dx=KW)
                                  ).then_inc(w_stack_ready, 1)
            pool.wait_ge(bias_in, 16)
            pool.wait_ge(w_stack_zero, 1)
            nc.gpsimd.tensor_copy(w_stack[:, 1, STACK:STACK + 1], bias_col[:]).then_inc(w_stack_ready, 1)
            nc.gpsimd.memset(x_pad[0:STACK, :, :, 0:PADW:PADW - 1], 0.0).then_inc(pad_ready, 1)
            pool.wait_ge(vareps_ready, 1)
            nc.gpsimd.tensor_tensor(stat[:, RSTD, :], stat[:, RSTD, :], minus_half[:], ALU.pow
                                    ).then_inc(rstd_ready, 1)
            pool.wait_ge(rstd_ready, 1)
            nc.gpsimd.memset(x_pad[STACK:P, :, :, :], 1.0).then_inc(pad_ready, 1)
            pool.wait_ge(pad_ready, 2)
            for r in range(ROUNDS):
                pool.wait_ge(norm_by_act, len(ACT_NORM) * (r + 1))
                pool.wait_ge(norm_by_dve, len(DVE_NORM) * (r + 1))
                if r:
                    pool.wait_ge(edge_zero, 2 * r)
                nc.gpsimd.memset(x_pad[0:C, quad_of(r), 0, 1:W + 1], 0.0).then_inc(edge_zero, 1)
                pool.wait_ge(edge_zero, 2 * r + 1)
                nc.gpsimd.memset(x_pad[2 * C:3 * C, quad_of(r), H - 1, 1:W + 1], 0.0).then_inc(edge_zero, 1)

        @block.scalar
        def _(act):
            act.dma_start(w1_rep[:], repeat(se_w1, 1, QUADS)
                          ).then_inc(w1_in, 16)
            act.dma_start(w2_ext[:, 0:HID], se_w2).then_inc(w2_in, 16)
            act.dma_start(w2_ext[:, HID:HID + 1], se_b2.rearrange("(k a) -> k a", a=1)).then_inc(w2_in, 16)
            act.dma_start(w_raw[:], w_dram).then_inc(w_in, 16)
            act.dma_start(bias_col[:], bias.rearrange("(n a) -> n a", a=1)).then_inc(bias_in, 16)
            nc.scalar.preload_act_table(ACT.Exp)
            for g in range(ROUNDS):
                act.wait_ge(nat_in[g], 16)
                nc.scalar.activation(y_sb[:, g, :], x_nat[:, g, :], ACT.Copy, accum_out=x_sum[:, g:g + 1]
                                     ).then_inc(sums_ready, 1)

            def normalise(r):
                act.wait_ge(raw_in[r], 16 * KH)
                for q in ACT_NORM:
                    b = QUADS * r + q
                    nc.scalar.activation(x_pad[0:STACK, b, :, 1:W + 1],
                                         x_raw[:, b, :].rearrange("p (h w) -> p h w", h=H), ACT.Identity,
                                         scale=stat_rep[:, RSTD, b:b + 1], bias=stat_rep[:, NBIAS, b:b + 1]
                                         ).then_inc(norm_by_act, 1)

            def evacuate(piece):
                dx, bs, cols = mix_cols(piece)
                act.wait_ge(mix_done, piece + 1)
                nc.scalar.activation(mixed[:, dx, bs, :], mix_ps[:, dx, cols], ACT.Copy).then_inc(mixed_by_act, 1)

            act.wait_ge(stat_done, 1)
            nc.scalar.activation(stat_rep[:], stat_ps, ACT.Copy).then_inc(stat_rep_ready, 1)
            act.wait_ge(stat_rep_ready, 1)
            act.wait_ge(raw_edge_ready, 2)
            act.wait_ge(below_top_ready, 1)
            nc.scalar.activation(e_all[:], below_top[:], ACT.Exp, scale=1.0 / TEMPERATURE).then_inc(e_ready, 1)
            normalise(0)
            normalise(1)
            for piece in (0, 2):
                evacuate(piece)
            normalise(2)
            for piece in (3, 5):
                evacuate(piece)
            normalise(3)

        @block.vector
        def _(dve):
            nc.vector.memset(x_raw[0:C, :, 0:W], 0.0).then_inc(raw_edge_ready, 1)
            nc.vector.memset(x_raw[2 * C:3 * C, :, PIX - W:PIX], 0.0).then_inc(raw_edge_ready, 1)
            dve.wait_ge(ident_ready, 1)
            nc.vector.tensor_reduce(diag_c[:], ident[:].rearrange("p (j c) -> p c j", c=C), AX_X, ALU.add
                                    ).then_inc(masks_ready, 1)
            nc.vector.tensor_reduce(in_quad[:], ident[:].rearrange("p (j c) -> p j c", c=C), AX_X, ALU.add
                                    ).then_inc(masks_ready, 1)
            nc.vector.tensor_copy(expert_rows[:].rearrange("k (e o) -> k e o", e=K),
                                  repeat(ident[0:K, 0:K], 2, O)).then_inc(masks_ready, 1)
            dve.wait_ge(masks_ready, 1)
            nc.vector.tensor_copy(pick_chan[:].rearrange("p (d c) -> p d c", d=KH),
                                  repeat(diag_c[:], 1, KH)).then_inc(masks_ready, 1)
            dve.wait_ge(w1t_done, 1)
            nc.vector.tensor_copy(w1_t[:], w1t_ps).then_inc(w1t_ready, 1)
            dve.wait_ge(w2t_done, 1)
            nc.vector.tensor_copy(w2_t[:], w2t_ps).then_inc(w2t_ready, 1)

            for g in range(ROUNDS):
                dve.wait_ge(nat_in[g], 16)
                nc.vector.bn_stats(bn_raw[:, g, :], x_nat[:, g, :]).then_inc(bn_ready, 1)
            for g in range(ROUNDS):
                dve.wait_ge(bn_ready, g + 1)
                nc.vector.bn_aggr(stat[:, MEAN:RSTD + 1, g], bn_raw[:, g, :]).then_inc(aggr_ready, 1)
            dve.wait_ge(aggr_ready, ROUNDS)
            nc.vector.tensor_scalar(stat[:, RSTD, :], stat[:, RSTD, :], GN_EPS, None, ALU.add
                                    ).then_inc(vareps_ready, 1)
            dve.wait_ge(sums_ready, ROUNDS)
            nc.vector.scalar_tensor_tensor(out=resid_mean[:], in0=x_sum[:], scalar=1.0 / PIX,
                                           in1=stat[:, MEAN, :], op0=ALU.mult, op1=ALU.subtract
                                           ).then_inc(chain, 1)
            dve.wait_ge(rstd_ready, 1)
            dve.wait_ge(chain, 1)
            nc.vector.tensor_tensor(stat[:, POOLED, :], resid_mean[:], stat[:, RSTD, :], ALU.mult).then_inc(chain, 1)
            nc.vector.scalar_tensor_tensor(out=stat[:, NBIAS, :], in0=stat[:, MEAN, :], scalar=-1.0,
                                           in1=stat[:, RSTD, :], op0=ALU.mult, op1=ALU.mult).then_inc(chain, 1)

            def spread(lo, hi, ready):
                n = (hi - lo) * ROUNDS
                nc.vector.tensor_tensor(
                    stat_by_quad[:, lo:hi, :, :].rearrange("p s g j -> p (s g) j"),
                    repeat(stat[:, lo:hi, :].rearrange("p s g -> p (s g)"), 2, QUADS),
                    repeat(in_quad[:], 1, n), ALU.mult).then_inc(ready, 1)

            dve.wait_ge(masks_ready, 4)
            dve.wait_ge(chain, 2)
            spread(POOLED, POOLED + 1, pooled_ready)
            dve.wait_ge(chain, 3)
            spread(MEAN, NBIAS + 1, stat_ready)

            dve.wait_ge(pool_consts, 3)
            dve.wait_ge(hidden_done, 1)
            nc.vector.tensor_scalar(hidden[0:HID, :], hidden_ps, 0.0, None, ALU.max).then_inc(hidden_ready, 1)
            dve.wait_ge(hidden_ready, 1)
            dve.wait_ge(w2t_ready, 1)
            nc.vector.tensor_tensor(hidden_w2[:], repeat(hidden[:], 1, K),
                                    w2_t[:].rearrange("h (k o) -> h k o", k=K)[:, :, 0:B], ALU.mult
                                    ).then_inc(hidden_w2_ready, 1)

            dve.wait_ge(logits_done, 1)
            nc.vector.tensor_reduce(top[:], logit_ps[:, 0:K * B].rearrange("p (k b) -> p b k", k=K), AX_X, ALU.max
                                    ).then_inc(chain, 1)
            dve.wait_ge(chain, 4)
            nc.vector.tensor_tensor(below_top[:], logits.rearrange("p (k b) -> p k b", b=B),
                                    repeat(top[:], 1, K + 1), ALU.subtract
                                    ).then_inc(below_top_ready, 1)

            def normalise(r):
                dve.wait_ge(raw_in[r], 16 * KH)
                for q in DVE_NORM:
                    b = QUADS * r + q
                    nc.vector.tensor_scalar(x_pad[0:STACK, b, :, 1:W + 1],
                                            x_raw[:, b, :].rearrange("p (h w) -> p h w", h=H),
                                            stat_rep[:, MEAN, b:b + 1], stat_rep[:, RSTD, b:b + 1],
                                            ALU.subtract, ALU.mult).then_inc(norm_by_dve, 1)

            def evacuate(piece):
                dx, bs, cols = mix_cols(piece)
                dve.wait_ge(mix_done, piece + 1)
                nc.vector.tensor_copy(mixed[:, dx, bs, :], mix_ps[:, dx, cols].rearrange("p (b o) -> p b o", o=O)
                                      ).then_inc(mixed_by_dve, 1)

            dve.wait_ge(stat_rep_ready, 1)
            dve.wait_ge(raw_edge_ready, 2)
            dve.wait_ge(e_ready, 1)
            for half in range(HALVES):
                bs = slice(BH * half, BH * (half + 1))
                nc.vector.tensor_tensor(attn_diag[:, bs, :], repeat(e_all[:, K, bs], 2, O),
                                        repeat(diag_c[:], 1, BH), ALU.mult).then_inc(diag_ready, 1)
            normalise(0)
            normalise(1)
            evacuate(1)
            normalise(2)
            evacuate(4)
            normalise(3)

            nc.vector.tensor_reduce(e_sum[:], e_all[:, 0:K, :].rearrange("p k b -> p b k"), AX_X, ALU.add
                                    ).then_inc(chain, 1)
            dve.wait_ge(chain, 5)
            nc.vector.reciprocal(e_rsum[:].rearrange("p g j -> p (g j)"), e_sum[:]).then_inc(chain, 1)
            dve.wait_ge(chain, 6)
            nc.vector.tensor_tensor(e_rsum_quad[:], e_rsum[:], repeat(in_quad[:], 1, ROUNDS), ALU.mult
                                    ).then_inc(chain, 1)
            dve.wait_ge(chain, 7)
            nc.vector.tensor_reduce(out_scale[:], e_rsum_quad[:], AX_X, ALU.add).then_inc(chain, 1)
            dve.wait_ge(chain, 8)

            for r in range(ROUNDS):
                dve.wait_ge(conv_done, r + 1)
                nc.vector.scalar_tensor_tensor(out=y_sb[:, r, :], in0=conv_ps[:, r, 0:PIX],
                                               scalar=out_scale[:, r:r + 1], in1=x_nat[:, r, :],
                                               op0=ALU.mult, op1=ALU.add).then_inc(y_ready, 1)

        @block.tensor
        def _(pe):
            pe.wait_ge(ident_ready, 1)
            pe.wait_ge(w1_in, 16)
            nc.tensor.matmul(w1t_ps, w1_rep[:].rearrange("n j c -> n (j c)"), ident[0:HID, 0:HID],
                             start=True, stop=True).then_inc(w1t_done, 1)
            pe.wait_ge(w2_in, 32)
            pe.wait_ge(masks_ready, 3)
            nc.tensor.matmul(w2t_ps, w2_ext[:], expert_rows[:], start=True, stop=True).then_inc(w2t_done, 1)
            pe.wait_ge(w1t_ready, 1)
            pe.wait_ge(pooled_ready, 1)
            nc.tensor.matmul(hidden_ps, w1_t[:], stat_by_quad[:, POOLED, :, :].rearrange("p g j -> p (g j)"),
                             start=True, stop=True).then_inc(hidden_done, 1)
            pe.wait_ge(masks_ready, 4)
            pe.wait_ge(stat_ready, 1)
            nc.tensor.matmul(stat_ps, pick_chan[:], stat_by_quad[:, MEAN:NBIAS + 1, :, :].rearrange(
                "p s g j -> p (s g j)"), start=True, stop=True).then_inc(stat_done, 1)
            pe.wait_ge(w2t_ready, 1)
            pe.wait_ge(hidden_ready, 1)
            nc.tensor.matmul(logit_ps[:, K * B:(K + 1) * B], w2_t[:], hidden[:], start=True, stop=True)
            pe.wait_ge(hidden_w2_ready, 1)
            nc.tensor.matmul(logit_ps[:, 0:K * B], ones[:], hidden_w2[:].rearrange("h k b -> h (k b)"),
                             start=True, stop=True).then_inc(logits_done, 1)
            pe.wait_ge(w_stack_ready, 2)
            for piece in range(HALVES * KW):
                dx, bs, cols = mix_cols(piece)
                if dx == 0:
                    pe.wait_ge(diag_ready, piece // KW + 1)
                if piece >= KW:
                    if evacuated_by_act(piece - KW):
                        pe.wait_ge(mixed_by_act, 1 + (piece - KW) // 2)
                    else:
                        pe.wait_ge(mixed_by_dve, 1)
                nc.tensor.matmul(mix_ps[:, dx, cols], w_stack[:, dx, :], attn_diag[:, bs, :].rearrange(
                    "p b o -> p (b o)"), start=True, stop=True).then_inc(mix_done, 1)
            pe.wait_ge(pad_ready, 2)
            for r in range(ROUNDS):
                half = r // (ROUNDS // HALVES)
                pe.wait_ge(edge_zero, 2 * (r + 1))
                pe.wait_ge(mixed_by_act, 2 * (half + 1))
                pe.wait_ge(mixed_by_dve, half + 1)
                for dx in range(KW):
                    for q in range(QUADS):
                        b = QUADS * r + q
                        last = nc.tensor.matmul(conv_ps[q * O:(q + 1) * O, r, 0:PIX], mixed[:, dx, b, :],
                                                x_pad[:, b, :, dx:dx + W], start=(dx == 0), stop=(dx == KW - 1))
                last.then_inc(conv_done, 1)


_INS = ["x", "L0_conv_weight", "L0_conv_bias", "L0_conv_se_w1", "L0_conv_se_w2", "L0_conv_se_b2"]


def kernel(**inputs):
    import numpy as np
    import concourse.bacc as bacc
    from concourse.bass_utils import run_bass_kernel_spmd

    nc = bacc.Bacc("TRN2", target_bir_lowering=False, num_devices=1)
    arrays, args = {}, []
    for name in _INS:
        a = np.ascontiguousarray(inputs[name])
        arrays[f"in_{name}"] = a
        args.append(nc.dram_tensor(f"in_{name}", a.shape, mybir.dt.from_np(a.dtype), kind="ExternalInput").ap())
    result = nc.dram_tensor("out_0", arrays["in_x"].shape, F32, kind="ExternalOutput").ap()
    preact_dynamic_conv(nc, *args, result)
    ran = run_bass_kernel_spmd(nc, [arrays], core_ids=[0])
    return ran.results[0]["out_0"]
```

```python
from contextlib import ExitStack

import concourse.bass as bass
from concourse import mybir

F32 = mybir.dt.float32
ALU = mybir.AluOpType
ACT = mybir.ActivationFunctionType
AX_X = mybir.AxisListType.X

GN_EPS = 1e-5
TEMPERATURE = 30.0
WARM = (14, 3, 5, 2, 8)


def repeat(ap, axis, n):
    longer = ap.unsqueeze(axis)
    shape = list(longer.shape)
    shape[axis] = n
    return longer.broadcast_to(shape)


def preact_dynamic_conv(nc: bass.Bass, x, weight, bias, se_w1, se_w2, se_b2, out):
    B, C, H, W = x.shape
    KO, _, KH, KW = weight.shape
    HID = se_w1.shape[0]
    K = se_w2.shape[0]
    O = KO // K
    PIX = H * W
    P = 128
    QUADS = P // C
    ROUNDS = B // QUADS
    STACK = KH * C
    PADW = W + 2
    HALVES = 2
    BH = B // HALVES
    assert C == 32 and O == 32 and KO == P and KH == 3 and KW == 3 and P % C == 0 and HID < 63

    x_nat_dram = x.rearrange("(g j) c h w -> (j c) g (h w)", g=ROUNDS)
    out_dram = out.rearrange("(g j) c h w -> (j c) g (h w)", g=ROUNDS)
    x_chan_dram = x.rearrange("b c h w -> c b (h w)")
    w_dram = weight.rearrange("n c kh kw -> n (c kh kw)")

    ctx = ExitStack()
    with ctx:
        def sb(name, shape):
            return ctx.enter_context(nc.sbuf_tensor(name, shape, F32))

        def pb(name, shape):
            return ctx.enter_context(nc.psum_tensor(name, shape, F32))

        def sem(name):
            return ctx.enter_context(nc.semaphore(name))

        x_nat = sb("x_nat", [P, ROUNDS, PIX])
        x_raw = sb("x_raw", [STACK, B, PIX])
        x_pad = sb("x_pad", [P, B, H, PADW])
        y_sb = sb("y_sb", [P, ROUNDS, PIX])
        w_raw = sb("w_raw", [P, C * KH * KW])
        bias_col = sb("bias_col", [P, 1])
        w1_rep = sb("w1_rep", [HID, QUADS, C])
        w2_ext = sb("w2_ext", [K, HID + 1])
        ident = sb("ident", [P, P])
        diag_c = sb("diag_c", [P, C])
        in_quad = sb("in_quad", [P, QUADS])
        pick_chan = sb("pick_chan", [P, STACK])
        expert_rows = sb("expert_rows", [K, P])
        ones = sb("ones", [HID + 1, P])
        minus_half = sb("minus_half", [P, ROUNDS])
        w_stack = sb("w_stack", [P, KW, P])
        w1_t = sb("w1_t", [P, HID])
        w2_t = sb("w2_t", [HID + 1, P])
        bn_raw = sb("bn_raw", [P, ROUNDS, 6])
        x_sum = sb("x_sum", [P, ROUNDS])
        MEAN, RSTD, NBIAS = range(3)
        stat = sb("stat", [P, 3, ROUNDS])
        resid_mean = sb("resid_mean", [P, ROUNDS])
        mean_by_quad = sb("mean_by_quad", [P, ROUNDS, QUADS])
        pooled_by_quad = sb("pooled_by_quad", [P, ROUNDS, QUADS])
        stat_by_quad = sb("stat_by_quad", [P, 3, ROUNDS, QUADS])
        stat_rep = sb("stat_rep", [STACK, 3, B])
        hidden = sb("hidden", [HID + 1, B])
        hidden_w2 = sb("hidden_w2", [HID + 1, K, B])
        top = sb("top", [P, B])
        below_top = sb("below_top", [P, K + 1, B])
        e_all = sb("e_all", [P, K + 1, B])
        e_sum = sb("e_sum", [P, B])
        e_rsum = sb("e_rsum", [P, ROUNDS, QUADS])
        e_rsum_quad = sb("e_rsum_quad", [P, ROUNDS, QUADS])
        out_scale = sb("out_scale", [P, ROUNDS])
        attn_diag = sb("attn_diag", [P, B, O])
        mixed = sb("mixed", [P, KW, B, O])

        mix_ps = pb("mix_ps", [P, KW, 512])
        conv_ps = pb("conv_ps", [P, ROUNDS, 512])
        logit_ps = pb("logit_ps", [P, 512])
        filler = ident[:].bitcast(mybir.dt.bfloat16)
        w1t_ps = conv_ps[:, 0, 0:HID]
        hidden_ps = conv_ps[0:HID, 0, 64:64 + B]
        w2t_ps = conv_ps[0:HID + 1, 1, 0:P]
        stat_ps = conv_ps[0:STACK, 2, 0:3 * B]
        logits = logit_ps[:, 0:(K + 1) * B]

        nat_in = [sem(f"nat_in{h}") for h in range(HALVES)]
        raw_in = [sem(f"raw_in{h}") for h in range(HALVES)]
        w1_in = sem("w1_in")
        w2_in = sem("w2_in")
        w_in = sem("w_in")
        bias_in = sem("bias_in")
        ident_zero = sem("ident_zero")
        ident_ready = sem("ident_ready")
        raw_edge_ready = sem("raw_edge_ready")
        pool_consts = sem("pool_consts")
        pad_ready = sem("pad_ready")
        w_stack_zero = sem("w_stack_zero")
        w_stack_ready = sem("w_stack_ready")
        masks_ready = sem("masks_ready")
        w1t_done = sem("w1t_done")
        w1t_ready = sem("w1t_ready")
        w2t_done = sem("w2t_done")
        w2t_ready = sem("w2t_ready")
        sums_ready = sem("sums_ready")
        bn_ready = sem("bn_ready")
        aggr_ready = sem("aggr_ready")
        vareps_ready = sem("vareps_ready")
        rstd_ready = sem("rstd_ready")
        chain = sem("chain")
        pooled_ready = sem("pooled_ready")
        stat_ready = sem("stat_ready")
        hidden_done = sem("hidden_done")
        stat_done = sem("stat_done")
        stat_rep_ready = sem("stat_rep_ready")
        hidden_ready = sem("hidden_ready")
        hidden_w2_ready = sem("hidden_w2_ready")
        hidden_w2_preset = sem("hidden_w2_preset")
        logits_done = sem("logits_done")
        below_top_ready = sem("below_top_ready")
        e_ready = sem("e_ready")
        diag_ready = sem("diag_ready")
        mix_done = sem("mix_done")
        mixed_by_act = sem("mixed_by_act")
        mixed_by_dve = sem("mixed_by_dve")
        norm_by_act = sem("norm_by_act")
        norm_by_dve = sem("norm_by_dve")
        edge_zero = sem("edge_zero")
        conv_done = sem("conv_done")
        y_ready = sem("y_ready")
        y_out = sem("y_out")

        def quad_of(r):
            return slice(QUADS * r, QUADS * (r + 1))

        def half_of(r):
            return r // (ROUNDS // HALVES)

        def load_raw(eng, half, dy):
            bs = slice(BH * half, BH * (half + 1))
            lo, hi = max(0, 1 - dy) * W, (H - max(0, dy - 1)) * W
            move = (dy - 1) * W
            eng.dma_start(x_raw[dy * C:(dy + 1) * C, bs, lo:hi],
                          x_chan_dram[:, bs, lo + move:hi + move]).then_inc(raw_in[half], 16)

        def evacuated_by_act(piece):
            return piece % KW != 1

        EACH_NORM = QUADS // 2

        def mix_cols(piece):
            half, dx = divmod(piece, KW)
            return dx, slice(BH * half, BH * (half + 1)), slice(BH * O * half, BH * O * (half + 1))

        block = ctx.enter_context(nc.Block())

        @block.sync
        def _(sp):
            for half in range(HALVES):
                gs = slice(ROUNDS // HALVES * half, ROUNDS // HALVES * (half + 1))
                sp.dma_start(x_nat[:, gs, :], x_nat_dram[:, gs, :]).then_inc(nat_in[half], 16)
            sp.dma_start(w1_rep[:], repeat(se_w1, 1, QUADS)).then_inc(w1_in, 16)
            sp.dma_start(w2_ext[:, 0:HID], se_w2).then_inc(w2_in, 16)
            load_raw(sp, 0, 0)
            sp.dma_start(w2_ext[:, HID:HID + 1], se_b2.rearrange("(k a) -> k a", a=1)).then_inc(w2_in, 16)
            load_raw(sp, 0, 1)
            load_raw(sp, 0, 2)
            sp.dma_start(w_raw[:], w_dram).then_inc(w_in, 16)
            load_raw(sp, 1, 0)
            sp.dma_start(bias_col[:], bias.rearrange("(n a) -> n a", a=1)).then_inc(bias_in, 16)
            for dy in range(1, KH):
                load_raw(sp, 1, dy)
            for r in range(ROUNDS):
                sp.wait_ge(y_ready, r + 1)
                sp.dma_start(out_dram[:, r, :], y_sb[:, r, :]).then_inc(y_out, 16)
            sp.wait_ge(y_out, 16 * ROUNDS)

        @block.gpsimd
        def _(pool):
            nc.gpsimd.memset(ident[:], 0.0).then_inc(ident_zero, 1)
            pool.wait_ge(ident_zero, 1)
            nc.gpsimd.affine_select(out=ident[:], in_=ident[:], compare_op=ALU.not_equal, fill=1.0, base=0,
                                    pattern=[[-1, P]], channel_multiplier=1).then_inc(ident_ready, 1)
            nc.gpsimd.memset(ones[:], 1.0).then_inc(pool_consts, 1)
            nc.gpsimd.memset(hidden[:], 1.0).then_inc(pool_consts, 1)
            nc.gpsimd.memset(minus_half[:], -0.5).then_inc(pool_consts, 1)
            nc.gpsimd.memset(w_stack[:, :, STACK:P], 0.0).then_inc(w_stack_zero, 1)
            nc.gpsimd.memset(x_pad[0:STACK, :, :, 0:PADW:PADW - 1], 0.0).then_inc(pad_ready, 1)
            pool.wait_ge(pad_ready, 1)
            nc.gpsimd.memset(x_pad[STACK:P, 0:BH, :, :], 1.0).then_inc(pad_ready, 1)
            pool.wait_ge(pad_ready, 2)
            pool.wait_ge(vareps_ready, 1)
            nc.gpsimd.tensor_tensor(stat[:, RSTD, :], stat[:, RSTD, :], minus_half[:], ALU.pow
                                    ).then_inc(rstd_ready, 1)
            pool.wait_ge(w_in, 16)
            nc.gpsimd.tensor_copy(w_stack[:, :, 0:STACK].rearrange("p dx (dy c) -> p dx dy c", dy=KH),
                                  w_raw[:].rearrange("p (c dy dx) -> p dx dy c", dy=KH, dx=KW)
                                  ).then_inc(w_stack_ready, 1)
            pool.wait_ge(bias_in, 16)
            pool.wait_ge(w_stack_zero, 1)
            nc.gpsimd.tensor_copy(w_stack[:, 1, STACK:STACK + 1], bias_col[:]).then_inc(w_stack_ready, 1)
            pool.wait_ge(w_stack_ready, 2)
            nc.gpsimd.memset(x_pad[STACK:P, BH:B, :, :], 1.0).then_inc(pad_ready, 1)
            pool.wait_ge(pad_ready, 3)
            for r in range(ROUNDS):
                pool.wait_ge(norm_by_act, EACH_NORM * (r + 1))
                pool.wait_ge(norm_by_dve, EACH_NORM * (r + 1))
                if r:
                    pool.wait_ge(edge_zero, 2 * r)
                nc.gpsimd.memset(x_pad[0:C, quad_of(r), 0, 1:W + 1], 0.0).then_inc(edge_zero, 1)
                pool.wait_ge(edge_zero, 2 * r + 1)
                nc.gpsimd.memset(x_pad[2 * C:3 * C, quad_of(r), H - 1, 1:W + 1], 0.0).then_inc(edge_zero, 1)

        @block.scalar
        def _(act):
            nc.scalar.preload_act_table(ACT.Exp)
            for g in range(ROUNDS):
                act.wait_ge(nat_in[half_of(g)], 16)
                nc.scalar.activation(y_sb[:, g, :], x_nat[:, g, :], ACT.Copy, accum_out=x_sum[:, g:g + 1]
                                     ).then_inc(sums_ready, 1)

            act.wait_ge(w1t_done, 1)
            nc.scalar.activation(w1_t[:], w1t_ps, ACT.Copy).then_inc(w1t_ready, 1)
            act.wait_ge(w2t_done, 1)
            nc.scalar.activation(w2_t[:], w2t_ps, ACT.Copy).then_inc(w2t_ready, 1)

            def normalise(*samples):
                for b in samples:
                    act.wait_ge(raw_in[b // BH], 16 * KH)
                    nc.scalar.activation(x_pad[0:STACK, b, :, 1:W + 1],
                                         x_raw[:, b, :].rearrange("p (h w) -> p h w", h=H), ACT.Identity,
                                         scale=stat_rep[:, RSTD, b:b + 1], bias=stat_rep[:, NBIAS, b:b + 1]
                                         ).then_inc(norm_by_act, 1)

            def evacuate(piece):
                dx, bs, cols = mix_cols(piece)
                act.wait_ge(mix_done, piece + 1)
                nc.scalar.activation(mixed[:, dx, bs, :], mix_ps[:, dx, cols], ACT.Copy).then_inc(mixed_by_act, 1)

            act.wait_ge(stat_done, 1)
            nc.scalar.activation(stat_rep[:], stat_ps, ACT.Copy).then_inc(stat_rep_ready, 1)
            act.wait_ge(stat_rep_ready, 1)
            act.wait_ge(raw_edge_ready, 2)
            normalise(0)
            act.wait_ge(below_top_ready, 1)
            nc.scalar.activation(e_all[:], below_top[:], ACT.Exp, scale=1.0 / TEMPERATURE).then_inc(e_ready, 1)
            normalise(2, 4)
            evacuate(0)
            normalise(6)
            evacuate(2)
            normalise(8)
            evacuate(3)
            normalise(10)
            evacuate(5)
            normalise(12, 14)

        @block.vector
        def _(dve):
            nc.vector.memset(x_raw[0:C, :, 0:W], 0.0).then_inc(raw_edge_ready, 1)
            nc.vector.memset(x_raw[2 * C:3 * C, :, PIX - W:PIX], 0.0).then_inc(raw_edge_ready, 1)
            dve.wait_ge(ident_ready, 1)
            nc.vector.tensor_reduce(diag_c[:], ident[:].rearrange("p (j c) -> p c j", c=C), AX_X, ALU.add
                                    ).then_inc(masks_ready, 1)
            nc.vector.tensor_reduce(in_quad[:], ident[:].rearrange("p (j c) -> p j c", c=C), AX_X, ALU.add
                                    ).then_inc(masks_ready, 1)
            nc.vector.tensor_copy(expert_rows[:].rearrange("k (e o) -> k e o", e=K),
                                  repeat(ident[0:K, 0:K], 2, O)).then_inc(masks_ready, 1)
            dve.wait_ge(masks_ready, 1)
            nc.vector.tensor_copy(pick_chan[:].rearrange("p (d c) -> p d c", d=KH),
                                  repeat(diag_c[:], 1, KH)).then_inc(masks_ready, 1)
            for g in range(ROUNDS):
                dve.wait_ge(nat_in[half_of(g)], 16)
                nc.vector.bn_stats(bn_raw[:, g, :], x_nat[:, g, :]).then_inc(bn_ready, 1)
            for g in range(ROUNDS):
                dve.wait_ge(bn_ready, g + 1)
                nc.vector.bn_aggr(stat[:, MEAN:RSTD + 1, g], bn_raw[:, g, :]).then_inc(aggr_ready, 1)
            dve.wait_ge(aggr_ready, ROUNDS)
            nc.vector.tensor_scalar(stat[:, RSTD, :], stat[:, RSTD, :], GN_EPS, None, ALU.add
                                    ).then_inc(vareps_ready, 1)
            dve.wait_ge(sums_ready, ROUNDS)
            nc.vector.scalar_tensor_tensor(out=resid_mean[:], in0=x_sum[:], scalar=1.0 / PIX,
                                           in1=stat[:, MEAN, :], op0=ALU.mult, op1=ALU.subtract
                                           ).then_inc(chain, 1)
            dve.wait_ge(masks_ready, 4)
            dve.wait_ge(chain, 1)
            nc.vector.tensor_tensor(mean_by_quad[:], repeat(resid_mean[:], 2, QUADS), repeat(in_quad[:], 1, ROUNDS),
                                    ALU.mult).then_inc(chain, 1)
            dve.wait_ge(rstd_ready, 1)
            dve.wait_ge(chain, 2)
            nc.vector.tensor_tensor(pooled_by_quad[:], mean_by_quad[:], repeat(stat[:, RSTD, :], 2, QUADS), ALU.mult
                                    ).then_inc(pooled_ready, 1)
            nc.vector.scalar_tensor_tensor(out=stat[:, NBIAS, :], in0=stat[:, MEAN, :], scalar=-1.0,
                                           in1=stat[:, RSTD, :], op0=ALU.mult, op1=ALU.mult).then_inc(chain, 1)

            dve.wait_ge(chain, 3)
            nc.vector.tensor_tensor(stat_by_quad[:].rearrange("p s g j -> p (s g) j"),
                                    repeat(stat[:].rearrange("p s g -> p (s g)"), 2, QUADS),
                                    repeat(in_quad[:], 1, 3 * ROUNDS), ALU.mult).then_inc(stat_ready, 1)

            dve.wait_ge(w2t_ready, 1)
            nc.vector.tensor_copy(hidden_w2[:], w2_t[:].rearrange("h (k o) -> h k o", k=K)[:, :, 0:B]
                                  ).then_inc(hidden_w2_preset, 1)
            dve.wait_ge(pool_consts, 3)
            dve.wait_ge(hidden_w2_preset, 1)
            dve.wait_ge(hidden_done, 1)
            nc.vector.scalar_tensor_tensor(out=hidden_w2[0:HID], in0=repeat(hidden_ps, 1, K), scalar=0.0,
                                           in1=w2_t[0:HID].rearrange("h (k o) -> h k o", k=K)[:, :, 0:B],
                                           op0=ALU.max, op1=ALU.mult).then_inc(hidden_w2_ready, 1)
            nc.vector.tensor_scalar(hidden[0:HID, :], hidden_ps, 0.0, None, ALU.max).then_inc(hidden_ready, 1)

            def normalise(*samples):
                for b in samples:
                    dve.wait_ge(raw_in[b // BH], 16 * KH)
                    nc.vector.tensor_scalar(x_pad[0:STACK, b, :, 1:W + 1],
                                            x_raw[:, b, :].rearrange("p (h w) -> p h w", h=H),
                                            stat_rep[:, MEAN, b:b + 1], stat_rep[:, RSTD, b:b + 1],
                                            ALU.subtract, ALU.mult).then_inc(norm_by_dve, 1)

            def evacuate(piece):
                dx, bs, cols = mix_cols(piece)
                dve.wait_ge(mix_done, piece + 1)
                nc.vector.tensor_copy(mixed[:, dx, bs, :], mix_ps[:, dx, cols].rearrange("p (b o) -> p b o", o=O)
                                      ).then_inc(mixed_by_dve, 1)

            dve.wait_ge(stat_rep_ready, 1)
            dve.wait_ge(raw_edge_ready, 2)
            normalise(1)
            dve.wait_ge(logits_done, 1)
            nc.vector.tensor_reduce(top[:], logit_ps[:, 0:K * B].rearrange("p (k b) -> p b k", k=K), AX_X, ALU.max
                                    ).then_inc(chain, 1)
            dve.wait_ge(chain, 4)
            nc.vector.tensor_tensor(below_top[:], logits.rearrange("p (k b) -> p k b", b=B),
                                    repeat(top[:], 1, K + 1), ALU.subtract
                                    ).then_inc(below_top_ready, 1)

            def diagonal(half):
                bs = slice(BH * half, BH * (half + 1))
                nc.vector.tensor_tensor(attn_diag[:, bs, :], repeat(e_all[:, K, bs], 2, O),
                                        repeat(diag_c[:], 1, BH), ALU.mult).then_inc(diag_ready, 1)

            normalise(3)
            dve.wait_ge(e_ready, 1)
            diagonal(0)
            diagonal(1)
            normalise(5, 7)
            evacuate(1)
            normalise(9)
            evacuate(4)
            normalise(11, 13, 15)

            nc.vector.tensor_reduce(e_sum[:], e_all[:, 0:K, :].rearrange("p k b -> p b k"), AX_X, ALU.add
                                    ).then_inc(chain, 1)
            dve.wait_ge(chain, 5)
            nc.vector.reciprocal(e_rsum[:].rearrange("p g j -> p (g j)"), e_sum[:]).then_inc(chain, 1)
            dve.wait_ge(chain, 6)
            nc.vector.tensor_tensor(e_rsum_quad[:], e_rsum[:], repeat(in_quad[:], 1, ROUNDS), ALU.mult
                                    ).then_inc(chain, 1)
            dve.wait_ge(chain, 7)
            nc.vector.tensor_reduce(out_scale[:], e_rsum_quad[:], AX_X, ALU.add).then_inc(chain, 1)
            dve.wait_ge(chain, 8)

            for r in range(ROUNDS):
                dve.wait_ge(conv_done, r + 1)
                nc.vector.scalar_tensor_tensor(out=y_sb[:, r, :], in0=conv_ps[:, r, 0:PIX],
                                               scalar=out_scale[:, r:r + 1], in1=x_nat[:, r, :],
                                               op0=ALU.mult, op1=ALU.add).then_inc(y_ready, 1)

        @block.tensor
        def _(pe):
            def keep_warm(n):
                for _ in range(n):
                    nc.tensor.matmul(mix_ps[:, KW - 1, 0:2 * P], filler[:, 0:P], filler, start=True, stop=True)

            pe.wait_ge(ident_ready, 1)
            keep_warm(WARM[0])
            pe.wait_ge(w1_in, 16)
            nc.tensor.matmul(w1t_ps, w1_rep[:].rearrange("n j c -> n (j c)"), ident[0:HID, 0:HID],
                             start=True, stop=True).then_inc(w1t_done, 1)
            keep_warm(WARM[1])
            pe.wait_ge(w2_in, 32)
            pe.wait_ge(masks_ready, 3)
            nc.tensor.matmul(w2t_ps, w2_ext[:], expert_rows[:], start=True, stop=True).then_inc(w2t_done, 1)
            keep_warm(WARM[2])
            pe.wait_ge(w1t_ready, 1)
            pe.wait_ge(pooled_ready, 1)
            nc.tensor.matmul(hidden_ps, w1_t[:], pooled_by_quad[:].rearrange("p g j -> p (g j)"),
                             start=True, stop=True).then_inc(hidden_done, 1)
            pe.wait_ge(masks_ready, 4)
            pe.wait_ge(stat_ready, 1)
            nc.tensor.matmul(stat_ps, pick_chan[:], stat_by_quad[:].rearrange(
                "p s g j -> p (s g j)"), start=True, stop=True).then_inc(stat_done, 1)
            keep_warm(WARM[3])
            pe.wait_ge(hidden_w2_ready, 1)
            nc.tensor.matmul(logit_ps[:, 0:K * B], ones[:], hidden_w2[:].rearrange("h k b -> h (k b)"),
                             start=True, stop=True)
            pe.wait_ge(w2t_ready, 1)
            pe.wait_ge(hidden_ready, 1)
            nc.tensor.matmul(logit_ps[:, K * B:(K + 1) * B], w2_t[:], hidden[:], start=True, stop=True
                             ).then_inc(logits_done, 1)
            keep_warm(WARM[4])
            pe.wait_ge(w_stack_ready, 2)
            for piece in range(HALVES * KW):
                dx, bs, cols = mix_cols(piece)
                if dx == 0:
                    pe.wait_ge(diag_ready, piece // KW + 1)
                if piece >= KW:
                    if evacuated_by_act(piece - KW):
                        pe.wait_ge(mixed_by_act, 1 + (piece - KW) // 2)
                    else:
                        pe.wait_ge(mixed_by_dve, 1)
                nc.tensor.matmul(mix_ps[:, dx, cols], w_stack[:, dx, :], attn_diag[:, bs, :].rearrange(
                    "p b o -> p (b o)"), start=True, stop=True).then_inc(mix_done, 1)
            pe.wait_ge(pad_ready, 3)
            for r in range(ROUNDS):
                half = half_of(r)
                pe.wait_ge(edge_zero, 2 * (r + 1))
                pe.wait_ge(mixed_by_act, 2 * (half + 1))
                pe.wait_ge(mixed_by_dve, half + 1)
                for dx in range(KW):
                    for q in range(QUADS):
                        b = QUADS * r + q
                        last = nc.tensor.matmul(conv_ps[q * O:(q + 1) * O, r, 0:PIX], mixed[:, dx, b, :],
                                                x_pad[:, b, :, dx:dx + W], start=(dx == 0), stop=(dx == KW - 1))
                last.then_inc(conv_done, 1)


_INS = ["x", "L0_conv_weight", "L0_conv_bias", "L0_conv_se_w1", "L0_conv_se_w2", "L0_conv_se_b2"]


def kernel(**inputs):
    import numpy as np
    import concourse.bacc as bacc
    from concourse.bass_utils import run_bass_kernel_spmd

    nc = bacc.Bacc("TRN2", target_bir_lowering=False, num_devices=1)
    arrays, args = {}, []
    for name in _INS:
        a = np.ascontiguousarray(inputs[name])
        arrays[f"in_{name}"] = a
        args.append(nc.dram_tensor(f"in_{name}", a.shape, mybir.dt.from_np(a.dtype), kind="ExternalInput").ap())
    result = nc.dram_tensor("out_0", arrays["in_x"].shape, F32, kind="ExternalOutput").ap()
    preact_dynamic_conv(nc, *args, result)
    ran = run_bass_kernel_spmd(nc, [arrays], core_ids=[0])
    return ran.results[0]["out_0"]
```

```python
from contextlib import ExitStack

import concourse.bass as bass
from concourse import mybir

F32 = mybir.dt.float32
ALU = mybir.AluOpType
ACT = mybir.ActivationFunctionType
AX_X = mybir.AxisListType.X

GN_EPS = 1e-5
TEMPERATURE = 30.0
WARM = (33, 5, 9, 4)


def repeat(ap, axis, n):
    longer = ap.unsqueeze(axis)
    shape = list(longer.shape)
    shape[axis] = n
    return longer.broadcast_to(shape)


def preact_dynamic_conv(nc: bass.Bass, x, weight, bias, se_w1, se_w2, se_b2, out):
    B, C, H, W = x.shape
    KO, _, KH, KW = weight.shape
    HID = se_w1.shape[0]
    K = se_w2.shape[0]
    O = KO // K
    PIX = H * W
    P = 128
    QUADS = P // C
    ROUNDS = B // QUADS
    STACK = KH * C
    PADW = W + 2
    HALVES = 2
    BH = B // HALVES
    RH = ROUNDS // HALVES
    assert C == 32 and O == 32 and KO == P and KH == 3 and KW == 3 and P % C == 0 and HID < 63

    x_nat_dram = x.rearrange("(g j) c h w -> (j c) g (h w)", g=ROUNDS)
    out_dram = out.rearrange("(g j) c h w -> (j c) g (h w)", g=ROUNDS)
    x_chan_dram = x.rearrange("b c h w -> c b (h w)")
    w_dram = weight.rearrange("n c kh kw -> n (c kh kw)")

    ctx = ExitStack()
    with ctx:
        def sb(name, shape):
            return ctx.enter_context(nc.sbuf_tensor(name, shape, F32))

        def pb(name, shape):
            return ctx.enter_context(nc.psum_tensor(name, shape, F32))

        def sem(name):
            return ctx.enter_context(nc.semaphore(name))

        x_nat = sb("x_nat", [P, ROUNDS, PIX])
        x_raw = sb("x_raw", [STACK, B, PIX])
        x_pad = sb("x_pad", [P, B, H, PADW])
        y_sb = sb("y_sb", [P, ROUNDS, PIX])
        w_raw = sb("w_raw", [P, C * KH * KW])
        bias_col = sb("bias_col", [P, 1])
        w1_rep = sb("w1_rep", [HID, QUADS, C])
        w2_ext = sb("w2_ext", [K, HID + 1])
        filler = sb("filler", [P, 1])
        ident = sb("ident", [P, P])
        diag_c = sb("diag_c", [P, C])
        in_quad = sb("in_quad", [P, QUADS])
        pick_chan = sb("pick_chan", [P, STACK])
        expert_rows = sb("expert_rows", [K, P])
        ones = sb("ones", [HID + 1, P])
        minus_half = sb("minus_half", [P, RH])
        w_stack = sb("w_stack", [P, KW, P])
        w1_t = sb("w1_t", [P, HID])
        w2_t = sb("w2_t", [HID + 1, P])
        bn_raw = sb("bn_raw", [P, ROUNDS, 6])
        x_sum = sb("x_sum", [P, ROUNDS])
        MEAN, RSTD, NBIAS = range(3)
        stat = sb("stat", [P, HALVES, 3, RH])
        resid_mean = sb("resid_mean", [P, ROUNDS])
        mean_by_quad = sb("mean_by_quad", [P, ROUNDS, QUADS])
        pooled_by_quad = sb("pooled_by_quad", [P, ROUNDS, QUADS])
        stat_by_quad = sb("stat_by_quad", [P, HALVES, 3 * RH, QUADS])
        stat_rep = sb("stat_rep", [STACK, HALVES, 3, BH])
        hidden = sb("hidden", [HID + 1, HALVES, BH])
        hidden_w2 = sb("hidden_w2", [HID + 1, HALVES, K, BH])
        top = sb("top", [P, HALVES, BH])
        below_top = sb("below_top", [P, HALVES, K + 1, BH])
        e_all = sb("e_all", [P, HALVES, K + 1, BH])
        e_sum = sb("e_sum", [P, HALVES, BH])
        e_rsum = sb("e_rsum", [P, ROUNDS, QUADS])
        e_rsum_quad = sb("e_rsum_quad", [P, ROUNDS, QUADS])
        out_scale = sb("out_scale", [P, ROUNDS])
        attn_diag = sb("attn_diag", [P, B, O])
        mixed = sb("mixed", [P, KW, B, O])

        mix_ps = pb("mix_ps", [P, KW, 512])
        conv_ps = pb("conv_ps", [P, ROUNDS, 512])
        logit_ps = pb("logit_ps", [P, 512])
        w1t_ps = conv_ps[:, 0, 0:HID]
        w2t_ps = conv_ps[0:HID + 1, 1, 0:P]
        hidden_ps = [conv_ps[0:HID, half, P:P + BH] for half in range(HALVES)]
        stat_ps = [conv_ps[0:STACK, HALVES + half, 0:3 * BH] for half in range(HALVES)]
        logits = [logit_ps[:, 0:(K + 1) * BH], conv_ps[:, HALVES, PIX:PIX + (K + 1) * BH]]

        nat_in = [sem(f"nat_in{h}") for h in range(HALVES)]
        raw_in = [sem(f"raw_in{h}") for h in range(HALVES)]
        w1_in = sem("w1_in")
        w2_in = sem("w2_in")
        w_in = sem("w_in")
        bias_in = sem("bias_in")
        filler_ready = sem("filler_ready")
        ident_zero = sem("ident_zero")
        ident_ready = sem("ident_ready")
        raw_edge_ready = sem("raw_edge_ready")
        pool_consts = sem("pool_consts")
        pad_ready = sem("pad_ready")
        first_ones_ready = sem("first_ones_ready")
        w_stack_zero = sem("w_stack_zero")
        w_stack_ready = sem("w_stack_ready")
        masks_ready = sem("masks_ready")
        w1t_done = sem("w1t_done")
        w1t_ready = sem("w1t_ready")
        w2t_done = sem("w2t_done")
        w2t_ready = sem("w2t_ready")
        sums_ready = sem("sums_ready")
        bn_ready = sem("bn_ready")
        aggr_ready = sem("aggr_ready")
        vareps_ready = sem("vareps_ready")
        rstd_ready = sem("rstd_ready")
        resid_ready = sem("resid_ready")
        mean_ready = sem("mean_ready")
        nbias_ready = sem("nbias_ready")
        top_ready = sem("top_ready")
        chain = sem("chain")
        pooled_ready = sem("pooled_ready")
        stat_ready = sem("stat_ready")
        hidden_done = sem("hidden_done")
        stat_done = sem("stat_done")
        stat_rep_ready = sem("stat_rep_ready")
        hidden_ready = sem("hidden_ready")
        hidden_w2_ready = sem("hidden_w2_ready")
        hidden_w2_preset = sem("hidden_w2_preset")
        logits_done = sem("logits_done")
        below_top_ready = sem("below_top_ready")
        e_ready = sem("e_ready")
        diag_ready = sem("diag_ready")
        mix_done = sem("mix_done")
        mixed_by_act = sem("mixed_by_act")
        mixed_by_dve = sem("mixed_by_dve")
        norm_by_act = sem("norm_by_act")
        norm_by_dve = sem("norm_by_dve")
        edge_zero = sem("edge_zero")
        conv_done = sem("conv_done")
        y_ready = sem("y_ready")
        y_out = sem("y_out")

        def quad_of(r):
            return slice(QUADS * r, QUADS * (r + 1))

        def half_of(r):
            return r // RH

        def rounds_of(half):
            return slice(RH * half, RH * (half + 1))


        def load_raw(eng, half, dy):
            bs = slice(BH * half, BH * (half + 1))
            lo, hi = max(0, 1 - dy) * W, (H - max(0, dy - 1)) * W
            move = (dy - 1) * W
            eng.dma_start(x_raw[dy * C:(dy + 1) * C, bs, lo:hi],
                          x_chan_dram[:, bs, lo + move:hi + move]).then_inc(raw_in[half], 16)

        def rep_of(which, b):
            return stat_rep[:, b // BH, which, b % BH:b % BH + 1]

        MIX_BANKS = KW + 1

        def evacuated_by_act(piece):
            return piece % KW != 1

        EACH_NORM = QUADS // 2

        def mix_part(piece):
            half, dx = divmod(piece, KW)
            return dx, slice(BH * half, BH * (half + 1))

        def mix_bank(piece):
            turn = piece % MIX_BANKS
            return (mix_ps[:, turn] if turn < KW else logit_ps)[:, 0:BH * O]

        block = ctx.enter_context(nc.Block())

        @block.sync
        def _(sp):
            for half in range(HALVES):
                sp.dma_start(x_nat[:, rounds_of(half), :], x_nat_dram[:, rounds_of(half), :]).then_inc(nat_in[half], 16)
            sp.dma_start(w1_rep[:], repeat(se_w1, 1, QUADS)).then_inc(w1_in, 16)
            sp.dma_start(w2_ext[:, 0:HID], se_w2).then_inc(w2_in, 16)
            sp.dma_start(w2_ext[:, HID:HID + 1], se_b2.rearrange("(k a) -> k a", a=1)).then_inc(w2_in, 16)
            sp.dma_start(w_raw[:], w_dram).then_inc(w_in, 16)
            load_raw(sp, 0, 0)
            sp.dma_start(bias_col[:], bias.rearrange("(n a) -> n a", a=1)).then_inc(bias_in, 16)
            for dy in range(1, KH):
                load_raw(sp, 0, dy)
            for dy in range(KH):
                load_raw(sp, 1, dy)
            for r in range(ROUNDS):
                sp.wait_ge(y_ready, r + 1)
                sp.dma_start(out_dram[:, r, :], y_sb[:, r, :]).then_inc(y_out, 16)
            sp.wait_ge(y_out, 16 * ROUNDS)

        @block.gpsimd
        def _(pool):
            nc.gpsimd.memset(ident[:], 0.0).then_inc(ident_zero, 1)
            pool.wait_ge(ident_zero, 1)
            nc.gpsimd.affine_select(out=ident[:], in_=ident[:], compare_op=ALU.not_equal, fill=1.0, base=0,
                                    pattern=[[-1, P]], channel_multiplier=1).then_inc(ident_ready, 1)
            nc.gpsimd.memset(ones[:], 1.0).then_inc(pool_consts, 1)
            nc.gpsimd.memset(hidden[:], 1.0).then_inc(pool_consts, 1)
            nc.gpsimd.memset(minus_half[:], -0.5).then_inc(pool_consts, 1)
            nc.gpsimd.memset(w_stack[:, :, STACK:P], 0.0).then_inc(w_stack_zero, 1)
            nc.gpsimd.memset(x_pad[0:STACK, :, :, 0:PADW:PADW - 1], 0.0).then_inc(pad_ready, 1)
            pool.wait_ge(pad_ready, 1)
            nc.gpsimd.memset(x_pad[STACK:P, QUADS:BH, :, :], 1.0).then_inc(pad_ready, 1)
            pool.wait_ge(pad_ready, 2)
            for half in range(HALVES):
                pool.wait_ge(vareps_ready, half + 1)
                nc.gpsimd.tensor_tensor(stat[:, half, RSTD, :], stat[:, half, RSTD, :], minus_half[:], ALU.pow
                                        ).then_inc(rstd_ready, 1)
            pool.wait_ge(rstd_ready, HALVES)
            nc.gpsimd.memset(x_pad[STACK:P, BH:B, :, :], 1.0).then_inc(pad_ready, 1)
            pool.wait_ge(pad_ready, 3)
            for r in range(ROUNDS):
                pool.wait_ge(norm_by_act, EACH_NORM * (r + 1))
                pool.wait_ge(norm_by_dve, EACH_NORM * (r + 1))
                if r:
                    pool.wait_ge(edge_zero, 2 * r)
                nc.gpsimd.memset(x_pad[0:C, quad_of(r), 0, 1:W + 1], 0.0).then_inc(edge_zero, 1)
                pool.wait_ge(edge_zero, 2 * r + 1)
                nc.gpsimd.memset(x_pad[2 * C:3 * C, quad_of(r), H - 1, 1:W + 1], 0.0).then_inc(edge_zero, 1)

        @block.scalar
        def _(act):
            nc.scalar.preload_act_table(ACT.Exp)
            for g in range(ROUNDS):
                act.wait_ge(nat_in[half_of(g)], 16)
                nc.scalar.activation(y_sb[:, g, :], x_nat[:, g, :], ACT.Copy, accum_out=x_sum[:, g:g + 1]
                                     ).then_inc(sums_ready, 1)

            act.wait_ge(w1t_done, 1)
            nc.scalar.activation(w1_t[:], w1t_ps, ACT.Copy).then_inc(w1t_ready, 1)
            act.wait_ge(w2t_done, 1)
            nc.scalar.activation(w2_t[:], w2t_ps, ACT.Copy).then_inc(w2t_ready, 1)

            act.wait_ge(w_in, 16)
            nc.scalar.activation(w_stack[:, :, 0:STACK].rearrange("p dx (dy c) -> p dx dy c", dy=KH),
                                 w_raw[:].rearrange("p (c dy dx) -> p dx dy c", dy=KH, dx=KW), ACT.Copy
                                 ).then_inc(w_stack_ready, 1)
            act.wait_ge(bias_in, 16)
            act.wait_ge(w_stack_zero, 1)
            nc.scalar.activation(w_stack[:, 1, STACK:STACK + 1], bias_col[:], ACT.Copy).then_inc(w_stack_ready, 1)

            def normalise(*samples):
                for b in samples:
                    act.wait_ge(raw_in[b // BH], 16 * KH)
                    nc.scalar.activation(x_pad[0:STACK, b, :, 1:W + 1],
                                         x_raw[:, b, :].rearrange("p (h w) -> p h w", h=H), ACT.Identity,
                                         scale=rep_of(RSTD, b), bias=rep_of(NBIAS, b)
                                         ).then_inc(norm_by_act, 1)

            def evacuate(piece):
                dx, bs = mix_part(piece)
                act.wait_ge(mix_done, piece + 1)
                nc.scalar.activation(mixed[:, dx, bs, :].rearrange("p b o -> p (b o)"), mix_bank(piece), ACT.Copy
                                     ).then_inc(mixed_by_act, 1)

            def stat_to_sbuf(half):
                act.wait_ge(stat_done, half + 1)
                nc.scalar.activation(stat_rep[:, half], stat_ps[half].rearrange("p (s b) -> p s b", s=3), ACT.Copy
                                     ).then_inc(stat_rep_ready, 1)

            def exponent(half):
                act.wait_ge(below_top_ready, half + 1)
                nc.scalar.activation(e_all[:, half], below_top[:, half], ACT.Exp, scale=1.0 / TEMPERATURE
                                     ).then_inc(e_ready, 1)

            stat_to_sbuf(0)
            exponent(0)
            stat_to_sbuf(1)
            act.wait_ge(stat_rep_ready, 1)
            act.wait_ge(raw_edge_ready, 2)
            normalise(0)
            exponent(1)
            normalise(2)
            evacuate(0)
            evacuate(2)
            normalise(4)
            evacuate(3)
            normalise(6)
            act.wait_ge(stat_rep_ready, 2)
            normalise(8)
            normalise(10)
            evacuate(5)
            normalise(12, 14)

        @block.vector
        def _(dve):
            nc.vector.memset(filler[:], 1.0).then_inc(filler_ready, 1)
            nc.vector.memset(x_raw[0:C, :, 0:W], 0.0).then_inc(raw_edge_ready, 1)
            nc.vector.memset(x_raw[2 * C:3 * C, :, PIX - W:PIX], 0.0).then_inc(raw_edge_ready, 1)
            dve.wait_ge(ident_ready, 1)
            nc.vector.tensor_reduce(diag_c[:], ident[:].rearrange("p (j c) -> p c j", c=C), AX_X, ALU.add
                                    ).then_inc(masks_ready, 1)
            nc.vector.tensor_reduce(in_quad[:], ident[:].rearrange("p (j c) -> p j c", c=C), AX_X, ALU.add
                                    ).then_inc(masks_ready, 1)
            nc.vector.tensor_copy(expert_rows[:].rearrange("k (e o) -> k e o", e=K),
                                  repeat(ident[0:K, 0:K], 2, O)).then_inc(masks_ready, 1)
            dve.wait_ge(masks_ready, 1)
            nc.vector.tensor_copy(pick_chan[:].rearrange("p (d c) -> p d c", d=KH),
                                  repeat(diag_c[:], 1, KH)).then_inc(masks_ready, 1)
            def image_stats(g):
                dve.wait_ge(nat_in[half_of(g)], 16)
                nc.vector.bn_stats(bn_raw[:, g, :], x_nat[:, g, :]).then_inc(bn_ready, 1)

            def moments(half):
                for g in range(RH * half, RH * (half + 1)):
                    dve.wait_ge(bn_ready, g + 1)
                    nc.vector.bn_aggr(stat[:, half, MEAN:RSTD + 1, g - RH * half], bn_raw[:, g, :]
                                      ).then_inc(aggr_ready, 1)

            def add_eps(half):
                dve.wait_ge(aggr_ready, RH * (half + 1))
                nc.vector.tensor_scalar(stat[:, half, RSTD, :], stat[:, half, RSTD, :], GN_EPS, None, ALU.add
                                        ).then_inc(vareps_ready, 1)

            def residual_mean(half):
                gs = rounds_of(half)
                dve.wait_ge(sums_ready, RH * (half + 1))
                nc.vector.scalar_tensor_tensor(out=resid_mean[:, gs], in0=x_sum[:, gs], scalar=1.0 / PIX,
                                               in1=stat[:, half, MEAN, :], op0=ALU.mult, op1=ALU.subtract
                                               ).then_inc(resid_ready, 1)

            def residual_by_quad(half):
                gs = rounds_of(half)
                dve.wait_ge(resid_ready, half + 1)
                nc.vector.tensor_tensor(mean_by_quad[:, gs], repeat(resid_mean[:, gs], 2, QUADS),
                                        repeat(in_quad[:], 1, RH), ALU.mult).then_inc(mean_ready, 1)

            def pooled_mean(half):
                gs = rounds_of(half)
                dve.wait_ge(rstd_ready, half + 1)
                dve.wait_ge(mean_ready, half + 1)
                nc.vector.tensor_tensor(pooled_by_quad[:, gs], mean_by_quad[:, gs],
                                        repeat(stat[:, half, RSTD, :], 2, QUADS), ALU.mult
                                        ).then_inc(pooled_ready, 1)

            def minus_mean_rstd(half):
                nc.vector.scalar_tensor_tensor(out=stat[:, half, NBIAS, :], in0=stat[:, half, MEAN, :], scalar=-1.0,
                                               in1=stat[:, half, RSTD, :], op0=ALU.mult, op1=ALU.mult
                                               ).then_inc(nbias_ready, 1)

            def stats_by_quad(half):
                dve.wait_ge(nbias_ready, half + 1)
                nc.vector.tensor_tensor(stat_by_quad[:, half],
                                        repeat(stat[:, half].rearrange("p s g -> p (s g)"), 2, QUADS),
                                        repeat(in_quad[:], 1, 3 * RH), ALU.mult).then_inc(stat_ready, 1)

            w2_by_expert = w2_t[:].rearrange("h (k o) -> h k o", k=K)[:, :, 0:BH]

            def rectify(half):
                dve.wait_ge(hidden_done, half + 1)
                nc.vector.tensor_scalar(hidden[0:HID, half], hidden_ps[half], 0.0, None, ALU.max
                                        ).then_inc(hidden_ready, 1)

            def weigh_hidden(half):
                nc.vector.scalar_tensor_tensor(out=hidden_w2[0:HID, half], in0=repeat(hidden_ps[half], 1, K),
                                               scalar=0.0, in1=w2_by_expert[0:HID],
                                               op0=ALU.max, op1=ALU.mult).then_inc(hidden_w2_ready, 1)

            def largest(half):
                dve.wait_ge(logits_done, half + 1)
                nc.vector.tensor_reduce(top[:, half], logits[half][:, 0:K * BH].rearrange(
                    "p (k b) -> p b k", k=K), AX_X, ALU.max).then_inc(top_ready, 1)

            def subtract_largest(half):
                dve.wait_ge(top_ready, half + 1)
                nc.vector.tensor_tensor(below_top[:, half], logits[half].rearrange("p (k b) -> p k b", b=BH),
                                        repeat(top[:, half], 1, K + 1), ALU.subtract
                                        ).then_inc(below_top_ready, 1)

            def diagonal(half):
                dve.wait_ge(e_ready, half + 1)
                for r in range(RH * half, RH * (half + 1)):
                    first = QUADS * (r - RH * half)
                    nc.vector.tensor_tensor(attn_diag[:, quad_of(r), :],
                                            repeat(e_all[:, half, K, first:first + QUADS], 2, O),
                                            repeat(diag_c[:], 1, QUADS), ALU.mult).then_inc(diag_ready, 1)

            def normalise(*samples):
                for b in samples:
                    dve.wait_ge(raw_in[b // BH], 16 * KH)
                    nc.vector.tensor_scalar(x_pad[0:STACK, b, :, 1:W + 1],
                                            x_raw[:, b, :].rearrange("p (h w) -> p h w", h=H),
                                            rep_of(MEAN, b), rep_of(RSTD, b),
                                            ALU.subtract, ALU.mult).then_inc(norm_by_dve, 1)

            def evacuate(piece):
                dx, bs = mix_part(piece)
                dve.wait_ge(mix_done, piece + 1)
                nc.vector.tensor_copy(mixed[:, dx, bs, :], mix_bank(piece).rearrange("p (b o) -> p b o", o=O)
                                      ).then_inc(mixed_by_dve, 1)

            nc.vector.memset(x_pad[STACK:P, 0:QUADS, :, :], 1.0).then_inc(first_ones_ready, 1)
            dve.wait_ge(masks_ready, 4)
            image_stats(0)
            image_stats(1)
            moments(0)
            add_eps(0)
            residual_mean(0)
            image_stats(2)
            residual_by_quad(0)
            image_stats(3)
            pooled_mean(0)
            moments(1)
            minus_mean_rstd(0)
            add_eps(1)
            stats_by_quad(0)
            residual_mean(1)
            residual_by_quad(1)
            dve.wait_ge(pool_consts, 3)
            rectify(0)
            dve.wait_ge(w2t_ready, 1)
            nc.vector.tensor_copy(hidden_w2[:], repeat(w2_by_expert, 1, HALVES)).then_inc(hidden_w2_preset, 1)
            dve.wait_ge(hidden_w2_preset, 1)
            weigh_hidden(0)
            pooled_mean(1)
            minus_mean_rstd(1)
            stats_by_quad(1)
            largest(0)
            rectify(1)
            subtract_largest(0)
            weigh_hidden(1)
            dve.wait_ge(stat_rep_ready, 1)
            dve.wait_ge(raw_edge_ready, 2)
            normalise(1)
            diagonal(0)
            largest(1)
            subtract_largest(1)
            normalise(3)
            diagonal(1)
            normalise(5)
            evacuate(1)
            normalise(7)
            dve.wait_ge(stat_rep_ready, 2)
            normalise(9)
            evacuate(4)
            normalise(11, 13, 15)

            for half in range(HALVES):
                nc.vector.tensor_reduce(e_sum[:, half], e_all[:, half, 0:K, :].rearrange("p k b -> p b k"),
                                        AX_X, ALU.add).then_inc(chain, 1)
            dve.wait_ge(chain, HALVES)
            nc.vector.reciprocal(e_rsum[:].rearrange("p g j -> p (g j)"),
                                 e_sum[:].rearrange("p h b -> p (h b)")).then_inc(chain, 1)
            dve.wait_ge(chain, HALVES + 1)
            nc.vector.tensor_tensor(e_rsum_quad[:], e_rsum[:], repeat(in_quad[:], 1, ROUNDS), ALU.mult
                                    ).then_inc(chain, 1)
            dve.wait_ge(chain, HALVES + 2)
            nc.vector.tensor_reduce(out_scale[:], e_rsum_quad[:], AX_X, ALU.add).then_inc(chain, 1)
            dve.wait_ge(chain, HALVES + 3)

            for r in range(ROUNDS):
                dve.wait_ge(conv_done, r + 1)
                nc.vector.scalar_tensor_tensor(out=y_sb[:, r, :], in0=conv_ps[:, r, 0:PIX],
                                               scalar=out_scale[:, r:r + 1], in1=x_nat[:, r, :],
                                               op0=ALU.mult, op1=ALU.add).then_inc(y_ready, 1)

        @block.tensor
        def _(pe):
            def keep_warm(n):
                for _ in range(n):
                    nc.tensor.matmul(mix_ps[:, KW - 1, 0:P], filler_bf16.broadcast_to([P, P]),
                                     filler_bf16.broadcast_to([P, P]), start=True, stop=True)

            filler_bf16 = filler[:].bitcast(mybir.dt.bfloat16)[:, 0:1]
            pe.wait_ge(filler_ready, 1)
            keep_warm(WARM[0])
            pe.wait_ge(ident_ready, 1)
            pe.wait_ge(w1_in, 16)
            nc.tensor.matmul(w1t_ps, w1_rep[:].rearrange("n j c -> n (j c)"), ident[0:HID, 0:HID],
                             start=True, stop=True).then_inc(w1t_done, 1)
            keep_warm(WARM[1])
            pe.wait_ge(w2_in, 32)
            pe.wait_ge(masks_ready, 3)
            nc.tensor.matmul(w2t_ps, w2_ext[:], expert_rows[:], start=True, stop=True).then_inc(w2t_done, 1)
            pe.wait_ge(w1t_ready, 1)
            pe.wait_ge(masks_ready, 4)

            def hidden_units(half):
                pe.wait_ge(pooled_ready, half + 1)
                nc.tensor.matmul(hidden_ps[half], w1_t[:], pooled_by_quad[:, rounds_of(half)].rearrange(
                    "p g j -> p (g j)"), start=True, stop=True).then_inc(hidden_done, 1)

            def stack_stats(half):
                pe.wait_ge(stat_ready, half + 1)
                nc.tensor.matmul(stat_ps[half], pick_chan[:], stat_by_quad[:, half].rearrange(
                    "p s j -> p (s j)"), start=True, stop=True).then_inc(stat_done, 1)

            def own_logit(half):
                if half:
                    pe.wait_ge(stat_rep_ready, 1)
                pe.wait_ge(hidden_ready, half + 1)
                nc.tensor.matmul(logits[half][:, K * BH:], w2_t[:], hidden[:, half], start=True, stop=True)

            def all_logits(half):
                pe.wait_ge(hidden_w2_ready, half + 1)
                nc.tensor.matmul(logits[half][:, 0:K * BH], ones[:], hidden_w2[:, half].rearrange(
                    "h k b -> h (k b)"), start=True, stop=True).then_inc(logits_done, 1)

            hidden_units(0)
            keep_warm(WARM[2])
            pe.wait_ge(w2t_ready, 1)
            own_logit(0)
            all_logits(0)
            stack_stats(0)
            hidden_units(1)
            stack_stats(1)
            own_logit(1)
            all_logits(1)
            keep_warm(WARM[3])
            pe.wait_ge(w_stack_ready, 2)
            for piece in range(HALVES * KW):
                dx, bs = mix_part(piece)
                if piece == 0:
                    for r in range(RH):
                        pe.wait_ge(diag_ready, r + 1)
                        at = QUADS * O * r
                        last = nc.tensor.matmul(mix_bank(0)[:, at:at + QUADS * O], w_stack[:, dx, :],
                                                attn_diag[:, quad_of(r), :].rearrange("p b o -> p (b o)"),
                                                start=True, stop=True)
                    last.then_inc(mix_done, 1)
                    continue
                if dx == 0:
                    pe.wait_ge(diag_ready, RH * (piece // KW + 1))
                if piece >= MIX_BANKS:
                    if evacuated_by_act(piece - MIX_BANKS):
                        pe.wait_ge(mixed_by_act, 1)
                    else:
                        pe.wait_ge(mixed_by_dve, 1)
                nc.tensor.matmul(mix_bank(piece), w_stack[:, dx, :], attn_diag[:, bs, :].rearrange(
                    "p b o -> p (b o)"), start=True, stop=True).then_inc(mix_done, 1)
            pe.wait_ge(first_ones_ready, 1)
            pe.wait_ge(pad_ready, 3)
            for r in range(ROUNDS):
                half = half_of(r)
                pe.wait_ge(edge_zero, 2 * (r + 1))
                pe.wait_ge(mixed_by_act, 2 * (half + 1))
                pe.wait_ge(mixed_by_dve, half + 1)
                for dx in range(KW):
                    for q in range(QUADS):
                        b = QUADS * r + q
                        last = nc.tensor.matmul(conv_ps[q * O:(q + 1) * O, r, 0:PIX], mixed[:, dx, b, :],
                                                x_pad[:, b, :, dx:dx + W], start=(dx == 0), stop=(dx == KW - 1))
                last.then_inc(conv_done, 1)


_INS = ["x", "L0_conv_weight", "L0_conv_bias", "L0_conv_se_w1", "L0_conv_se_w2", "L0_conv_se_b2"]


def kernel(**inputs):
    import numpy as np
    import concourse.bacc as bacc
    from concourse.bass_utils import run_bass_kernel_spmd

    nc = bacc.Bacc("TRN2", target_bir_lowering=False, num_devices=1)
    arrays, args = {}, []
    for name in _INS:
        a = np.ascontiguousarray(inputs[name])
        arrays[f"in_{name}"] = a
        args.append(nc.dram_tensor(f"in_{name}", a.shape, mybir.dt.from_np(a.dtype), kind="ExternalInput").ap())
    result = nc.dram_tensor("out_0", arrays["in_x"].shape, F32, kind="ExternalOutput").ap()
    preact_dynamic_conv(nc, *args, result)
    ran = run_bass_kernel_spmd(nc, [arrays], core_ids=[0])
    return ran.results[0]["out_0"]
```
